# Optimizing a Trainium2 kernel written in Bass

```python
import numpy as np
import jax
import jax.numpy as jnp

def _softmax(x, axis=-1):
    return jax.nn.softmax(x, axis=axis)

def _gelu(x):
    return jax.nn.gelu(x, approximate=True)

def _silu(x):
    return jax.nn.silu(x)

def _sigmoid(x):
    return jax.nn.sigmoid(x)

def _layernorm(x, axis=-1, eps=1e-05):
    m = jnp.mean(x, axis=axis, keepdims=True)
    v = jnp.var(x, axis=axis, keepdims=True)
    return (x - m) / jnp.sqrt(v + eps)

def _scatter_add(tgt, idx, src, axis=0):
    return tgt.at[idx].add(src)

def _segment_sum(src, seg, n):
    return jax.ops.segment_sum(src, seg, n)
kernel_name = 'mk_seq_preln_d1_jaxref_r4_2fe606'

def setup_inputs(seed: int=0):
    np.random.seed(seed)
    _w = jnp.asarray

    def _L0_attn_setup():
        import jax, jax.numpy as jnp
        import numpy as np
        from jax import lax
        H = 1024
        DIN = 2048
        N = 16
        K = 4
        R = 64
        B_SZ = 2
        L = 512
        EPS = 1e-06

        def rmsnorm(x, w):
            return x * lax.rsqrt(jnp.mean(x * x, axis=-1, keepdims=True) + EPS) * w

        def _selective_scan(x, dt, A, Bm, Cm):
            xT = jnp.transpose(x, (2, 0, 1))
            dtT = jnp.transpose(dt, (2, 0, 1))
            BT = jnp.transpose(Bm, (2, 0, 1))
            CT = jnp.transpose(Cm, (2, 0, 1))

            def step(h, inp):
                x_t, dt_t, B_t, C_t = inp
                dA = jnp.exp(dt_t[..., None] * A)
                dBx = dt_t[..., None] * B_t[:, None, :] * x_t[..., None]
                h = dA * h + dBx
                y = jnp.einsum('bdn,bn->bd', h, C_t)
                return (h, y)
            h0 = jnp.zeros((x.shape[0], x.shape[1], A.shape[1]), dtype=x.dtype)
            _, ys = lax.scan(step, h0, (xT, dtT, BT, CT))
            return jnp.transpose(ys, (1, 2, 0))
        key = jax.random.key(seed)
        ks = jax.random.split(key, 8)
        hidden_states = jax.random.normal(ks[0], (B_SZ, L, H), dtype=jnp.float32)
        s = 0.02
        in_proj_w = jax.random.normal(ks[1], (H, 2 * DIN), dtype=jnp.float32) * s
        conv_w = jax.random.normal(ks[2], (DIN, K), dtype=jnp.float32) * 0.2
        conv_b = jax.random.normal(ks[3], (DIN,), dtype=jnp.float32) * 0.02
        x_proj_w = jax.random.normal(ks[4], (R + 2 * N, DIN), dtype=jnp.float32) * s
        dt_proj_w = jax.random.normal(ks[5], (DIN, R), dtype=jnp.float32) * s
        dt_bias = jax.random.normal(ks[6], (DIN,), dtype=jnp.float32) * 0.5 - 4.0
        A_log = jnp.log(jnp.broadcast_to(jnp.arange(1, N + 1, dtype=jnp.float32)[None, :], (DIN, N)))
        D_param = jnp.ones((DIN,), dtype=jnp.float32)
        out_proj_w = jax.random.normal(ks[7], (H, DIN), dtype=jnp.float32) * s
        dt_ln_w = jnp.ones((R,), dtype=jnp.float32)
        B_ln_w = jnp.ones((N,), dtype=jnp.float32)
        C_ln_w = jnp.ones((N,), dtype=jnp.float32)
        return dict(hidden_states=hidden_states, in_proj_w=in_proj_w, conv_w=conv_w, conv_b=conv_b, x_proj_w=x_proj_w, dt_proj_w=dt_proj_w, dt_bias=dt_bias, A_log=A_log, D_param=D_param, out_proj_w=out_proj_w, dt_ln_w=dt_ln_w, B_ln_w=B_ln_w, C_ln_w=C_ln_w)
    _L0_attn_in = _L0_attn_setup()

    def _L0_ffn_setup():
        import jax, jax.numpy as jnp
        import numpy as np
        BLOCK = 32

        def _dequantize(q_scales, q_vals):
            OUT, n_blocks = q_scales.shape
            codes = q_vals.astype(jnp.float32) - 128.0
            w = q_scales[:, :, None] * codes
            return w.reshape(OUT, n_blocks * BLOCK)
        key = jax.random.key(seed)
        k1, k2, k3, k4 = jax.random.split(key, 4)
        B, S, IN, OUT = (2, 1024, 1024, 1024)
        n_blocks = IN // BLOCK
        x = jax.random.normal(k1, (B, S, IN), dtype=jnp.float32)
        q_scales = jax.random.uniform(k2, (OUT, n_blocks), dtype=jnp.float32) * 0.05
        q_vals = jax.random.randint(k3, (OUT, n_blocks, BLOCK), 0, 64, dtype=jnp.int32)
        bias = jax.random.normal(k4, (OUT,), dtype=jnp.float32)
        return {'x': x, 'q_scales': q_scales, 'q_vals': q_vals, 'bias': bias}
    _L0_ffn_in = _L0_ffn_setup()
    _d = {'L0_attn_hidden_states': _L0_attn_in['hidden_states'], 'L0_attn_in_proj_w': _L0_attn_in['in_proj_w'], 'L0_attn_conv_w': _L0_attn_in['conv_w'], 'L0_attn_conv_b': _L0_attn_in['conv_b'], 'L0_attn_x_proj_w': _L0_attn_in['x_proj_w'], 'L0_attn_dt_proj_w': _L0_attn_in['dt_proj_w'], 'L0_attn_dt_bias': _L0_attn_in['dt_bias'], 'L0_attn_A_log': _L0_attn_in['A_log'], 'L0_attn_D_param': _L0_attn_in['D_param'], 'L0_attn_out_proj_w': _L0_attn_in['out_proj_w'], 'L0_attn_dt_ln_w': _L0_attn_in['dt_ln_w'], 'L0_attn_B_ln_w': _L0_attn_in['B_ln_w'], 'L0_attn_C_ln_w': _L0_attn_in['C_ln_w'], 'L0_ffn_q_scales': _L0_ffn_in['q_scales'], 'L0_ffn_q_vals': _L0_ffn_in['q_vals'], 'L0_ffn_bias': _L0_ffn_in['bias']}
    _x0 = _d['L0_attn_hidden_states']
    _d['L0_attn_hidden_states'] = jax.random.normal(jax.random.fold_in(jax.random.key(seed), 1), (1, 4096, 1024), dtype=_x0.dtype)
    del _x0
    return _d

def reference(L0_attn_hidden_states, L0_attn_in_proj_w, L0_attn_conv_w, L0_attn_conv_b, L0_attn_x_proj_w, L0_attn_dt_proj_w, L0_attn_dt_bias, L0_attn_A_log, L0_attn_D_param, L0_attn_out_proj_w, L0_attn_dt_ln_w, L0_attn_B_ln_w, L0_attn_C_ln_w, L0_ffn_q_scales, L0_ffn_q_vals, L0_ffn_bias):

    def _L0_attn_ref(hidden_states, in_proj_w, conv_w, conv_b, x_proj_w, dt_proj_w, dt_bias, A_log, D_param, out_proj_w, dt_ln_w, B_ln_w, C_ln_w):
        import jax, jax.numpy as jnp
        import numpy as np
        from jax import lax
        H = 1024
        DIN = 2048
        N = 16
        K = 4
        R = 64
        B_SZ = 2
        L = 512
        EPS = 1e-06

        def rmsnorm(x, w):
            return x * lax.rsqrt(jnp.mean(x * x, axis=-1, keepdims=True) + EPS) * w

        def _selective_scan(x, dt, A, Bm, Cm):
            xT = jnp.transpose(x, (2, 0, 1))
            dtT = jnp.transpose(dt, (2, 0, 1))
            BT = jnp.transpose(Bm, (2, 0, 1))
            CT = jnp.transpose(Cm, (2, 0, 1))

            def step(h, inp):
                x_t, dt_t, B_t, C_t = inp
                dA = jnp.exp(dt_t[..., None] * A)
                dBx = dt_t[..., None] * B_t[:, None, :] * x_t[..., None]
                h = dA * h + dBx
                y = jnp.einsum('bdn,bn->bd', h, C_t)
                return (h, y)
            h0 = jnp.zeros((x.shape[0], x.shape[1], A.shape[1]), dtype=x.dtype)
            _, ys = lax.scan(step, h0, (xT, dtT, BT, CT))
            return jnp.transpose(ys, (1, 2, 0))
        proj = hidden_states @ in_proj_w
        x, z = jnp.split(proj, 2, axis=-1)
        x = jnp.transpose(x, (0, 2, 1))
        z = jnp.transpose(z, (0, 2, 1))
        Lq = x.shape[-1]
        xp = jnp.pad(x, ((0, 0), (0, 0), (K - 1, 0)))
        xc = conv_b[None, :, None]
        for k in range(K):
            xc = xc + conv_w[None, :, k:k + 1] * xp[:, :, k:k + Lq]
        xc = jax.nn.silu(xc)
        ssm_p = jnp.einsum('bdl,ed->ble', xc, x_proj_w)
        dt_r = rmsnorm(ssm_p[..., :R], dt_ln_w)
        Bm = rmsnorm(ssm_p[..., R:R + N], B_ln_w)
        Cm = rmsnorm(ssm_p[..., R + N:], C_ln_w)
        dt = jnp.einsum('blr,dr->bdl', dt_r, dt_proj_w)
        dt = jax.nn.softplus(dt + dt_bias[None, :, None])
        A = -jnp.exp(A_log)
        Bm = jnp.transpose(Bm, (0, 2, 1))
        Cm = jnp.transpose(Cm, (0, 2, 1))
        ys = _selective_scan(xc, dt, A, Bm, Cm)
        y = (ys + D_param[None, :, None] * xc) * jax.nn.silu(z)
        return jnp.einsum('bdl,hd->blh', y, out_proj_w)

    def _L0_ffn_ref(x, q_scales, q_vals, bias):
        import jax, jax.numpy as jnp
        import numpy as np
        BLOCK = 32

        def _dequantize(q_scales, q_vals):
            OUT, n_blocks = q_scales.shape
            codes = q_vals.astype(jnp.float32) - 128.0
            w = q_scales[:, :, None] * codes
            return w.reshape(OUT, n_blocks * BLOCK)
        W = _dequantize(q_scales, q_vals)
        out = jnp.einsum('bsi,oi->bso', x, W) + bias
        return out
    x = L0_attn_hidden_states
    x = x + _L0_attn_ref(_layernorm(x, axis=-1), L0_attn_in_proj_w, L0_attn_conv_w, L0_attn_conv_b, L0_attn_x_proj_w, L0_attn_dt_proj_w, L0_attn_dt_bias, L0_attn_A_log, L0_attn_D_param, L0_attn_out_proj_w, L0_attn_dt_ln_w, L0_attn_B_ln_w, L0_attn_C_ln_w)
    x = x + _L0_ffn_ref(_layernorm(x, axis=-1), L0_ffn_q_scales, L0_ffn_q_vals, L0_ffn_bias)
    return x

_drawn_inputs = setup_inputs


def setup_inputs(seed=0):
    import zlib

    import numpy as np

    out = dict(_drawn_inputs(seed))
    spreads = {'L0_attn_D_param': (1.0, 0.6),
     'L0_attn_dt_ln_w': (1.0, 0.6),
     'L0_attn_B_ln_w': (1.0, 0.6),
     'L0_attn_C_ln_w': (1.0, 0.6)}
    factors = {'L0_attn_conv_b': 8.0,
     'L0_attn_x_proj_w': 4.049,
     'L0_attn_dt_proj_w': 8.0,
     'L0_attn_dt_bias': 8.0,
     'L0_attn_A_log': 7.312,
     'L0_ffn_bias': 2.833}
    for name, (base, spread) in spreads.items():
        noise = np.random.default_rng([zlib.crc32(name.encode()), seed]).standard_normal(out[name].shape)
        drawn = base * np.exp(spread * noise) if base else spread * noise
        out[name] = jnp.asarray(drawn.astype(out[name].dtype))
    for name, factor in factors.items():
        out[name] = (out[name] * factor).astype(out[name].dtype)
    return out
```

```python
from contextlib import ExitStack

import concourse.bass as bass
from concourse import mybir

ALU = mybir.AluOpType
ACT = mybir.ActivationFunctionType
AX = mybir.AxisListType
F32 = mybir.dt.float32
I32 = mybir.dt.int32
ds = bass.ds

P = 128
L, H, DIN, N, R, KC = 4096, 1024, 2048, 16, 64, 4
QB = 32
T = 256
NC = L // T
TT = T // P
KH = H // P
PAIRS = DIN // (2 * P)
TILES = DIN // P
E = R + 2 * N
NQ = 4
GW = NQ * T
HALF = GW // 2
EPS_LN = 1e-5
EPS_RMS = 1e-6
ZERO_POINT = 128.0


class Stages:

    def __init__(self, c, looped=False):
        self.c = c
        self.scan = looped or 0 <= c < NC
        self.inproj = looped or 0 <= c + 1 < NC
        self.outproj = looped or 0 <= c - 1 < NC
        self.ffn = looped or 0 <= c - 2 < NC
        self.norm1 = looped or 0 <= c + 2 < NC

    def g0_jobs(self, first, last):
        jobs = []
        if self.inproj:
            jobs.append("x")
        if self.inproj if last else self.scan:
            jobs.append("z")
        if self.inproj:
            jobs.append("xp")
        if first and self.ffn:
            jobs += ["l2t1", "l2t3"]
        if last and self.norm1:
            jobs += ["l1t1", "l1t3"]
        if last and self.inproj:
            jobs.append("nt")
        return jobs

    def g1_jobs(self, first, last):
        jobs = []
        if self.scan and not last:
            jobs.append("dt")
        if self.outproj:
            jobs += ["o", "ot"]
        if first and self.ffn:
            jobs += ["l2t0", "l2t2"]
        if last and self.norm1:
            jobs += ["l1t0", "l1t2"]
        if self.ffn:
            jobs.append("f")
        if last and self.inproj:
            jobs.append("dt")
        return jobs

    def per_iteration(self, jobs):
        return (len(jobs(True, False)) + (PAIRS - 2) * len(jobs(False, False))
                + len(jobs(False, True)))


def after(n):
    return max(n, 0) + 1 if isinstance(n, int) else n + 1


def landed(n):
    return 16 * after(n)


LOOP = range(2, NC - 2)


def bank_base(c, bank):
    def uses(i):
        s = Stages(i)
        return s.per_iteration(s.g0_jobs if bank == 0 else s.g1_jobs)

    before = 2
    i = -1
    while i < (LOOP[0] if not isinstance(c, int) else c):
        before += uses(i)
        i += 1
    return before if isinstance(c, int) else before + uses(LOOP[0]) * (c - LOOP[0])


def iterations(eng, body):
    for c in range(-1, LOOP[0]):
        body(Stages(c), c)
    with eng.Fori(LOOP[0], LOOP[-1] + 1) as c:
        body(Stages(c, looped=True), c)
    for c in range(LOOP[-1] + 1, NC + 2):
        body(Stages(c), c)


def steps(eng, step):
    step(0, True, False)
    with eng.Fori(1, PAIRS - 1) as j:
        step(j, False, False)
    step(PAIRS - 1, False, True)


def build_program(nc, x, win, wout, wf_codes, wf_scales, ffn_bias, xproj, dtw_in, convw_in, convb_in,
                  dtb_in, alog_in, dparam_in, lnw_in, out):
    ctx = ExitStack()
    with ctx:
        def sb(name, shape, dt=F32):
            return ctx.enter_context(nc.sbuf_tensor(name, shape, dt))

        def pb(name, shape):
            return ctx.enter_context(nc.psum_tensor(name, shape, F32))

        sems = []

        def sem(name):
            sems.append(ctx.enter_context(nc.semaphore(name)))
            return sems[-1]

        dma_sems = []

        def dsem(name):
            dma_sems.append(ctx.enter_context(nc.semaphore(name)))
            return dma_sems[-1]

        xc_dram = nc.dram_tensor("xc_scratch", (NC * PAIRS, P, 2 * T), F32, kind="Internal").ap()
        wf_dram = nc.dram_tensor("wf_scratch", (KH, P, KH * P), F32, kind="Internal").ap()
        bc_dram = nc.dram_tensor("bc_scratch", (NC, 2 * N, T), F32, kind="Internal").ap()

        wx = sb("wx", [P, KH, 2 * P])
        wz = sb("wz", [P, KH, 2 * P])
        wo = sb("wo", [P, TILES, P])
        wf = sb("wf", [P, KH, P])
        dtw = sb("dtw", [R, 2 * P])
        xprojw = sb("xprojw", [P, TILES, E])
        a_neg = sb("a_neg", [P, TILES * N])
        convw = sb("convw", [P, TILES * KC])
        convb = sb("convb", [P, TILES])
        dtb = sb("dtb", [P, TILES])
        dparam = sb("dparam", [P, TILES])
        lnw = sb("lnw", [E, 1])
        biasb = sb("biasb", [P, H])
        ident = sb("ident", [P, P])
        eps_ln = sb("eps_ln", [P, 1])
        eps_rms = sb("eps_rms", [P, 1])
        hstate = sb("hstate", [P, TILES * N])
        xhist = sb("xhist", [P, TILES, KC - 1])
        xrow = sb("xrow", [P, TT, H])
        xnT = sb("xnT", [P, 2, KH, T])
        bst1 = sb("bst1", [P, TT, 12])
        mv1 = sb("mv1", [P, TT, 2])
        rstd1 = sb("rstd1", [P, TT])
        bst2 = sb("bst2", [P, TT, 12])
        mv2 = sb("mv2", [P, TT, 2])
        rstd2 = sb("rstd2", [P, TT])
        xpre = sb("xpre", [P, 2, T + KC - 1])
        xcn = sb("xcn", [P, 2 * T])
        ux = sb("ux", [P, 2 * T])
        ssm = sb("ssm", [P, TT, E])
        ssn = sb("ssn", [P, TT, E])
        ssq = sb("ssq", [P, 6])
        ssmT = sb("ssmT", [E, T])
        ud = sb("ud", [P, 2 * T])
        ld = sb("ld", [P, 2 * T])
        dt = sb("dt", [P, 2, 2 * T])
        dtx = sb("dtx", [P, 2 * T])
        gate = sb("gate", [P, 2, 2 * T])
        uz = sb("uz", [P, 2 * T])
        xcs = sb("xcs", [P, 2, 2 * T])
        bb = sb("bb", [P, N, T])
        cb = sb("cb", [P, N, T])
        dbx = sb("dbx", [P, 2, GW])
        hc = sb("hc", [P, 2, GW])
        half = sb("half", [P, 2, HALF])
        scr = sb("scr", [P, 2 * T])
        ybuf = sb("ybuf", [P, 2 * PAIRS, 2 * T])
        ostage = sb("ostage", [P, T])
        x2 = sb("x2", [P, 2, TT * H])
        x2nT = sb("x2nT", [P, KH, T])

        dA = pb("dA", [P, GW])
        hps = pb("hps", [P, GW])
        ysum = pb("ysum", [P, 2 * 2 * T])
        g0 = pb("g0", [P, 2 * T])
        g1 = pb("g1", [P, 2 * T])

        consts_in, xrow_in, xres_in, out_st = dsem("consts_in"), dsem("xrow_in"), dsem("xres_in"), dsem("out_st")
        wx_in, wz_in, wo_in, wf_in, dtw_in_s = dsem("wx_in"), dsem("wz_in"), dsem("wo_in"), dsem("wf_in"), dsem("dtw_in_s")
        xc_st, xc_in, bc_st = dsem("xc_st"), dsem("xc_in"), dsem("bc_st")
        bb_in = [dsem(f"bb_in{q}") for q in range(NQ)]
        cb_in = [dsem(f"cb_in{q}") for q in range(NQ)]
        codes_in, scales_in, wf_st = dsem("codes_in"), dsem("scales_in"), dsem("wf_st")
        x_mm, z_mm, o_mm, f_mm, xp_mm, dt_mm = (sem("x_mm"), sem("z_mm"), sem("o_mm"), sem("f_mm"),
                                                sem("xp_mm"), sem("dt_mm"))
        o_tr, ss_tr, l1_tr, l2_tr, sum_mm = sem("o_tr"), sem("ss_tr"), sem("l1_tr"), sem("l2_tr"), sem("sum_mm")
        g0_free, g1_free = sem("g0_free"), sem("g1_free")
        x_evac, tap0, ux_act, sx_act = sem("x_evac"), sem("tap0"), sem("ux_act"), sem("sx_act")
        o_evac, z_evac, uz_act, sz_act = sem("o_evac"), sem("z_evac"), sem("uz_act"), sem("sz_act")
        dt_evac, ld_act, exps = sem("dt_evac"), sem("ld_act"), sem("exps")
        rms_ln, rms_r, ss_evac = sem("rms_ln"), sem("rms_r"), sem("ss_evac")
        l1_ln, l1_r, l1_evac, l2_ln, l2_r, l2_evac = (sem("l1_ln"), sem("l1_r"), sem("l1_evac"),
                                                      sem("l2_ln"), sem("l2_r"), sem("l2_evac"))
        a_exp, hist_read = sem("a_exp"), sem("hist_read")
        conv, mx_dve, xc_ready, scans, hstates, hcs = (sem("conv"), sem("mx_dve"), sem("xc_ready"), sem("scans"),
                                                       sem("hstates"), sem("hcs"))
        dt_dve, dt_ready, mz_dve, gate_ready, y_ready = (sem("dt_dve"), sem("dt_ready"), sem("mz_dve"),
                                                         sem("gate_ready"), sem("y_ready"))
        y_dve = sem("y_dve")
        x2_add, xp_add, f_add = sem("x2_add"), sem("xp_add"), sem("f_add")
        rms_dve, rms_ready, l1_dve, l1_stats, l1_ready, l2_dve, l2_stats, l2_ready = (
            sem("rms_dve"), sem("rms_ready"), sem("l1_dve"), sem("l1_stats"), sem("l1_ready"), sem("l2_dve"),
            sem("l2_stats"), sem("l2_ready"))
        aggr_go = sem("aggr_go")
        ssm_clear, bias_add = sem("ssm_clear"), sem("bias_add")
        deq_a, deq_b, a_ready = sem("deq_a"), sem("deq_b"), sem("a_ready")
        dbxs, halves, dtx_ready, id_zero, id_ready, zeroed = (sem("dbxs"), sem("halves"), sem("dtx_ready"),
                                                              sem("id_zero"), sem("id_ready"), sem("zeroed"))

        with nc.Block() as first_units:
            @first_units.sync
            def _(sp):
                for s in sems:
                    sp.sem_inc(s, 1)
                for s in dma_sems:
                    sp.sem_inc(s, 16)

        x_rows = x.rearrange("(c t p) h -> c p t h", p=P, t=TT)
        out_rows = out.rearrange("(c t p) h -> c p t h", p=P, t=TT)
        codes = ybuf[:, 0:2, :].rearrange("p a t -> p (a t)").bitcast(I32)
        scales = ybuf[:, 2:4, :].rearrange("p a t -> p (a t)")
        dequant = ybuf[:, 4:6, :].rearrange("p a t -> p (a t)")

        block = ctx.enter_context(nc.Block())

        @block.sync
        def _(sp):
            with nc.allow_non_contiguous_dma(reason="short rows of small weights, once"):
                sp.dma_start(xrow[:], x_rows[0]).then_inc(xrow_in, 16)
                for dst, src in ((xprojw[:].rearrange("p a b -> p (a b)"), xproj), (a_neg[:], alog_in),
                                 (convw[:], convw_in), (convb[:], convb_in), (dtb[:], dtb_in),
                                 (dparam[:], dparam_in), (lnw[:], lnw_in),
                                 (biasb[:], ffn_bias.partition_broadcast(P))):
                    sp.dma_start(dst, src).then_inc(consts_in, 16)

            def iteration(st, c):
                if st.scan and not st.inproj:
                    sp.wait_ge(xc_st, landed(NC * PAIRS))
                if st.outproj:
                    sp.wait_ge(out_st, landed(c - 2))
                    sp.dma_start(x2[:, (c + 1) % 2, :].rearrange("p (t h) -> p t h", t=TT),
                                 x_rows[c - 1]).then_inc(xres_in, 16)

                def step(j, first, last):
                    S = c * PAIRS + j
                    zz = st.inproj if last else st.scan
                    jn = 0 if last else j + 1
                    if st.inproj:
                        sp.wait_ge(x_mm, after(S + PAIRS))
                        sp.dma_start(wx[:].rearrange("p a b -> p (a b)"), win[j]).then_inc(wx_in, 16)
                    if zz:
                        sp.wait_ge(dt_mm, after(S + 1))
                        sp.dma_start(dtw[:], dtw_in[jn]).then_inc(dtw_in_s, 16)
                        sp.wait_ge(z_mm, after(S + 1))
                        sp.dma_start(wz[:].rearrange("p a b -> p (a b)"), win[jn + PAIRS]).then_inc(wz_in, 16)
                    if st.outproj:
                        sp.wait_ge(o_mm, after(S - PAIRS))
                        sp.dma_start(wo[:].rearrange("p a b -> p (a b)"), wout[j]).then_inc(wo_in, 16)
                    if st.ffn:
                        sp.wait_ge(wf_st, landed(KH))
                        sp.wait_ge(f_mm, after(S - 2 * PAIRS))
                        sp.dma_start(wf[:].rearrange("p a b -> p (a b)"), wf_dram[j]).then_inc(wf_in, 16)
                    if isinstance(c, int) and c == -1:
                        sp.wait_ge(deq_b, after(j))
                        sp.dma_start(codes, wf_codes[j]).then_inc(codes_in, 16)
                        for b in range(P // QB):
                            sp.dma_start(scales[b * QB:(b + 1) * QB, :],
                                         wf_scales[j, b:b + 1, :].to_broadcast([QB, KH * P])
                                         ).then_inc(scales_in, 16)
                        sp.wait_ge(deq_b, after(j + 1))
                        sp.dma_start(wf_dram[j], dequant).then_inc(wf_st, 16)
                    if zz:
                        sp.wait_ge(y_ready, after(S))
                        sp.dma_start(xcs[:, (S + 1) % 2, :], xc_dram[S + 1]).then_inc(xc_in, 16)
                    if st.inproj:
                        sp.wait_ge(xc_ready, after(S + PAIRS + 1))
                        sp.dma_start(xc_dram[S + PAIRS], xcn[:]).then_inc(xc_st, 16)
                    if first and st.norm1:
                        sp.wait_ge(l1_tr, after(4 * (c + 2)))
                        sp.wait_ge(l2_tr, after(4 * (c - 1)))
                        sp.dma_start(xrow[:], x_rows[c + 2]).then_inc(xrow_in, 16)
                    if last and st.inproj:
                        sp.wait_ge(ss_evac, after(c + 2))
                        sp.dma_start(bc_dram[c + 1], ssmT[R:E, :]).then_inc(bc_st, 16)
                        sp.wait_ge(bc_st, landed(c + 2))
                        for q in range(NQ):
                            if st.scan:
                                sp.wait_ge(dbxs, after(8 * S + NQ + q + 1))
                            sp.dma_start(bb[:, NQ * q:NQ * (q + 1), :].rearrange("p n t -> p (n t)"),
                                         bc_dram[c + 1, NQ * q:NQ * (q + 1), :].rearrange("n t -> (n t)")
                                         .partition_broadcast(P)).then_inc(bb_in[q], 16)
                            if st.scan:
                                sp.wait_ge(hcs, after(8 * S + NQ + q + 1))
                            sp.dma_start(cb[:, NQ * q:NQ * (q + 1), :].rearrange("p n t -> p (n t)"),
                                         bc_dram[c + 1, N + NQ * q:N + NQ * (q + 1), :].rearrange("n t -> (n t)")
                                         .partition_broadcast(P)).then_inc(cb_in[q], 16)
                    if last and st.ffn:
                        sp.wait_ge(f_add, after(S - 2 * PAIRS + 1))
                        sp.dma_start(out_rows[c - 2], x2[:, c % 2, :].rearrange("p (t h) -> p t h", t=TT)
                                     ).then_inc(out_st, 16)

                steps(sp, step)

            iterations(sp, iteration)
            sp.wait_ge(out_st, landed(NC))

        @block.gpsimd
        def _(pool):
            nc.gpsimd.memset(ident[:], 0.0).then_inc(id_zero, 1)
            nc.gpsimd.memset(eps_ln[:], EPS_LN).then_inc(zeroed, 1)
            nc.gpsimd.memset(eps_rms[:], EPS_RMS).then_inc(zeroed, 1)
            nc.gpsimd.memset(hstate[:], 0.0).then_inc(zeroed, 1)
            nc.gpsimd.memset(xhist[:], 0.0).then_inc(zeroed, 1)
            nc.gpsimd.memset(ssm[:], 0.0).then_inc(zeroed, 1)
            pool.wait_ge(id_zero, after(1))
            nc.gpsimd.affine_select(out=ident[:], in_=ident[:], compare_op=ALU.not_equal, fill=1.0, base=0,
                                    pattern=[[-1, P]], channel_multiplier=1).then_inc(id_ready, 1)

            def group_of_b(S, k, chunk):
                a, q = divmod(k, NQ)
                pool.wait_ge(scans, after(16 * S + 2 * (k - 1)))
                pool.wait_ge(bb_in[q], landed(chunk + 1))
                if k == 0:
                    pool.wait_ge(dtx_ready, after(S + 1))
                nc.gpsimd.tensor_tensor(
                    dbx[:, k % 2, :].rearrange("p (n t) -> p n t", n=NQ),
                    dtx[:, a * T:(a + 1) * T].unsqueeze(1).to_broadcast([P, NQ, T]),
                    bb[:, NQ * q:NQ * (q + 1), :], ALU.mult).then_inc(dbxs, 1)

            def group_sum(S, k):
                pool.wait_ge(hcs, after(8 * S + k + 1))
                pool.wait_ge(sum_mm, after(8 * S + k - 1))
                nc.gpsimd.tensor_tensor(half[:, k % 2, :], hc[:, k % 2, 0:HALF], hc[:, k % 2, HALF:GW],
                                        ALU.add).then_inc(halves, 1)

            def iteration(st, c):
                def step(j, first, last):
                    S = c * PAIRS + j
                    zz = st.inproj if last else st.scan
                    if st.scan:
                        for k in range(1, 8):
                            group_of_b(S, k, c)
                            group_sum(S, k - 1)
                    if zz:
                        pool.wait_ge(dt_ready, after(S + 2))
                        pool.wait_ge(xc_in, landed(S + 2))
                        pool.wait_ge(dbxs, after(8 * (S + 1)))
                        nc.gpsimd.tensor_tensor(dtx[:], dt[:, (S + 1) % 2, :], xcs[:, (S + 1) % 2, :],
                                                ALU.mult).then_inc(dtx_ready, 1)
                        group_of_b(S + 1, 0, c + 1 if last else c)
                    if st.scan:
                        group_sum(S, 7)

                if st.scan or st.inproj:
                    if st.scan:
                        steps(pool, step)
                    else:
                        step(PAIRS - 1, False, True)

            iterations(pool, iteration)

        @block.tensor
        def _(pe):
            def bank(st, c, j, first, last, which, job):
                jobs = st.g0_jobs if which == 0 else st.g1_jobs
                n_first, n_mid = len(jobs(True, False)), len(jobs(False, False))
                in_step = jobs(first, last).index(job)
                before = 0 if first else n_first + n_mid * (j - 1)
                pe.wait_ge(g0_free if which == 0 else g1_free, after(bank_base(c, which) + before + in_step))

            def transposes(src, tt, i, g, done):
                for m in range(4):
                    kk = 4 * (i % 2) + m
                    mm = nc.tensor.transpose(g[:, m * P:(m + 1) * P], src[:, tt, kk * P:(kk + 1) * P], ident[:])
                mm.then_inc(done, 1)

            pe.wait_ge(id_ready, after(1))
            pe.wait_ge(l1_ready, after(1))
            for i in range(4):
                if i >= 2:
                    pe.wait_ge((g1_free, g0_free)[i % 2], after(1))
                transposes(xrow, i // 2, i, (g1, g0)[i % 2], l1_tr)

            def iteration(st, c):
                def step(j, first, last):
                    S = c * PAIRS + j
                    zz = st.inproj if last else st.scan

                    def use(which, job):
                        bank(st, c, j, first, last, which, job)

                    def group(k):
                        if not st.scan:
                            return
                        a, q = divmod(k, NQ)
                        pe.wait_ge(halves, after(8 * S + k + 1))
                        if k == 0:
                            pe.wait_ge(y_ready, after(S - 1))
                        for i in range(2):
                            mm = nc.tensor.matmul(ysum[:, ds((S % 2) * 2 * T + a * T, T)], ident[:],
                                                  half[:, k % 2, i * T:(i + 1) * T],
                                                  start=(q == 0 and i == 0), stop=(q == NQ - 1 and i == 1))
                        mm.then_inc(sum_mm, 1)

                    def in_proj(w, chunk, job, done):
                        use(0, job)
                        for a in range(2):
                            for kk in range(KH):
                                mm = nc.tensor.matmul(g0[:, a * T:(a + 1) * T], w[:, kk, a * P:(a + 1) * P],
                                                      xnT[:, chunk % 2, kk, :], start=(kk == 0), stop=(kk == KH - 1))
                        mm.then_inc(done, 1)

                    def dt_proj():
                        use(1, "dt")
                        pe.wait_ge(dtw_in_s, landed(S + 2))
                        pe.wait_ge(ss_evac, after(c + 2 if last else c + 1))
                        for a in range(2):
                            mm = nc.tensor.matmul(g1[:, a * T:(a + 1) * T], dtw[:, a * P:(a + 1) * P], ssmT[0:R, :],
                                                  start=True, stop=True)
                        mm.then_inc(dt_mm, 1)

                    if st.inproj:
                        pe.wait_ge(wx_in, landed(S + PAIRS + 1))
                        pe.wait_ge(l1_evac, after(4 * (c + 2)))
                        in_proj(wx, c + 1, "x", x_mm)
                    group(0)
                    if zz:
                        if not last:
                            dt_proj()
                        pe.wait_ge(wz_in, landed(S + 2))
                        in_proj(wz, c + 1 if last else c, "z", z_mm)
                    group(1)
                    group(2)
                    if st.outproj:
                        pe.wait_ge(wo_in, landed(S - PAIRS + 1))
                        pe.wait_ge(y_ready, after(c * PAIRS))
                        use(1, "o")
                        for kt in range(TILES):
                            mm = nc.tensor.matmul(g1[:, 0:T], wo[:, kt, :],
                                                  ybuf[:, ds(((c + 1) % 2) * PAIRS + kt // 2, 1),
                                                       (kt % 2) * T:(kt % 2 + 1) * T],
                                                  start=(kt == 0), stop=(kt == TILES - 1))
                        mm.then_inc(o_mm, 1)
                    group(3)
                    group(4)
                    if st.outproj:
                        use(1, "ot")
                        pe.wait_ge(o_evac, after(S - PAIRS + 1))
                        for tt in range(TT):
                            mm = nc.tensor.transpose(g1[:, tt * P:(tt + 1) * P], ostage[:, tt * P:(tt + 1) * P],
                                                     ident[:])
                        mm.then_inc(o_tr, 1)
                    if st.inproj:
                        use(0, "xp")
                        pe.wait_ge(xc_ready, after(S + PAIRS + 1))
                        for tt in range(TT):
                            for a in range(2):
                                mm = nc.tensor.matmul(g0[:, tt * E:(tt + 1) * E],
                                                      xcn[:, a * T + tt * P:a * T + (tt + 1) * P],
                                                      xprojw[:, 2 * j + a, :], start=(a == 0), stop=(a == 1))
                        mm.then_inc(xp_mm, 1)
                    if first and st.ffn:
                        pe.wait_ge(l2_ready, after(c - 1))
                        for i in range(4):
                            use(1 - i % 2, f"l2t{i}")
                            transposes(xrow, i // 2, i, (g1, g0)[i % 2], l2_tr)
                    if last and st.norm1:
                        pe.wait_ge(l1_ready, after(c + 3))
                        for i in range(4):
                            use(1 - i % 2, f"l1t{i}")
                            transposes(xrow, i // 2, i, (g1, g0)[i % 2], l1_tr)
                    group(5)
                    if st.ffn:
                        pe.wait_ge(wf_in, landed(S - 2 * PAIRS + 1))
                        pe.wait_ge(l2_evac, after(4 * (c - 1)))
                        use(1, "f")
                        for tt in range(TT):
                            for kk in range(KH):
                                mm = nc.tensor.matmul(g1[:, tt * P:(tt + 1) * P], x2nT[:, kk, tt * P:(tt + 1) * P],
                                                      wf[:, kk, :], start=(kk == 0), stop=(kk == KH - 1))
                        mm.then_inc(f_mm, 1)
                    group(6)
                    if last and st.inproj:
                        pe.wait_ge(rms_ready, after(c + 2))
                        use(0, "nt")
                        for tt in range(TT):
                            mm = nc.tensor.transpose(g0[0:E, tt * P:(tt + 1) * P], ssn[:, tt, :], ident[:])
                        mm.then_inc(ss_tr, 1)
                        dt_proj()
                    group(7)

                steps(pe, step)

            iterations(pe, iteration)

        @block.scalar
        def _(act):
            nc.scalar.preload_act_table_set("natural_log_exp_and_others")
            act.wait_ge(consts_in, landed(8))
            nc.scalar.activation(a_neg[:], a_neg[:], ACT.Exp).then_inc(a_exp, 1)
            act.wait_ge(zeroed, after(5))

            def rstd(mv, r, stats, ln, ready, n):
                act.wait_ge(stats, after(n))
                nc.scalar.activation(r[:], mv[:, :, 1], ACT.Ln, bias=eps_ln[:]).then_inc(ln, 1)
                act.wait_ge(ln, after(n))
                nc.scalar.activation(r[:], r[:], ACT.Exp, scale=-0.5).then_inc(ready, 1)

            def norm_evac(dst, n, tr, evac):
                for i in range(4):
                    act.wait_ge(tr, after(n + i + 1))
                    nc.scalar.copy(dst[:, 4 * (i % 2):4 * (i % 2) + 4, (i // 2) * P:(i // 2 + 1) * P],
                                   (g1, g0)[i % 2][:].rearrange("p (k t) -> p k t", k=4)).then_inc(evac, 1)
                    act.wait_ge(evac, after(n + i + 1))
                    act.sem_inc((g1_free, g0_free)[i % 2], 1)

            rstd(mv1, rstd1, l1_stats, l1_ln, l1_r, 1)
            norm_evac(xnT[:, 0], 0, l1_tr, l1_evac)

            def iteration(st, c):
                def step(j, first, last):
                    S = c * PAIRS + j
                    SX = S + PAIRS
                    SN = S + 1
                    zz = st.inproj if last else st.scan
                    jn = 0 if last else j + 1

                    def group(k):
                        if not st.scan:
                            return
                        a, q = divmod(k, NQ)
                        if k == 0:
                            act.wait_ge(dt_ready, after(S + 1))
                            act.wait_ge(a_ready, after(1))
                        for b in range(2):
                            act.wait_ge(scans, after(16 * S + 2 * k + b - 1))
                            for i in range(2):
                                n = NQ * q + 2 * b + i
                                at = (2 * b + i) * T
                                ins = nc.scalar.activation(dA[:, at:at + T], dt[:, S % 2, a * T:(a + 1) * T], ACT.Exp,
                                                           scale=a_neg[:, ds((2 * j + a) * N + n, 1)])
                            ins.then_inc(exps, 1)

                    def x_taps():
                        act.wait_ge(x_mm, after(SX + 1))
                        act.wait_ge(conv, after(6 * SX))
                        nc.scalar.copy(xpre[:, :, 0:KC - 1], xhist[:, ds(2 * j, 2), :]).then_inc(hist_read, 1)
                        act.wait_ge(hist_read, after(SX + 1))
                        g = g0[:].rearrange("p (a t) -> p a t", a=2)
                        nc.scalar.copy(xpre[:, :, KC - 1:], g)
                        nc.scalar.copy(xhist[:, ds(2 * j, 2), :], g[:, :, T - KC + 1:T]).then_inc(x_evac, 1)
                        act.wait_ge(x_evac, after(SX + 1))
                        act.sem_inc(g0_free, 1)
                        act.wait_ge(xp_mm, after(SX))
                        act.wait_ge(xc_st, landed(SX))
                        for a in range(2):
                            ins = nc.scalar.activation(xcn[:, a * T:(a + 1) * T], xpre[:, a, 0:T], ACT.Identity,
                                                       bias=convb[:, ds(2 * j + a, 1)],
                                                       scale=convw[:, ds((2 * j + a) * KC, 1)])
                        ins.then_inc(tap0, 1)

                    def x_sigmoid():
                        act.wait_ge(conv, after(6 * SX + 6))
                        act.wait_ge(xc_ready, after(SX))
                        nc.scalar.activation(ux[:], xcn[:], ACT.Abs).then_inc(ux_act, 1)
                        act.wait_ge(ux_act, after(3 * SX + 1))
                        nc.scalar.activation(ux[:], ux[:], ACT.Exp, scale=-1.0).then_inc(ux_act, 1)
                        act.wait_ge(ux_act, after(3 * SX + 2))
                        nc.scalar.activation(ux[:], ux[:], ACT.Ln, bias=1.0).then_inc(ux_act, 1)

                    def dt_softplus():
                        act.wait_ge(dt_mm, after(SN + 1))
                        act.wait_ge(dt_ready, after(SN))
                        act.wait_ge(dtx_ready, after(SN - 1))
                        for a in range(2):
                            b = dtb[:, ds(2 * jn + a, 1)]
                            g = g1[:, a * T:(a + 1) * T]
                            nc.scalar.activation(ud[:, a * T:(a + 1) * T], g, ACT.Abs, bias=b)
                            ins = nc.scalar.activation(dt[:, SN % 2, a * T:(a + 1) * T], g, ACT.Relu, bias=b)
                        ins.then_inc(dt_evac, 1)
                        act.wait_ge(dt_evac, after(SN + 1))
                        act.sem_inc(g1_free, 1)
                        nc.scalar.activation(ud[:], ud[:], ACT.Exp, scale=-1.0).then_inc(ld_act, 1)
                        act.wait_ge(ld_act, after(2 * SN + 1))
                        nc.scalar.activation(ld[:], ud[:], ACT.Ln, bias=1.0).then_inc(ld_act, 1)

                    def z_sigmoid():
                        act.wait_ge(z_mm, after(SN + 1))
                        act.wait_ge(y_ready, after(SN - 1))
                        act.wait_ge(gate_ready, after(SN))
                        nc.scalar.copy(gate[:, SN % 2, :], g0[:])
                        nc.scalar.activation(uz[:], g0[:], ACT.Abs).then_inc(z_evac, 1)
                        act.wait_ge(z_evac, after(SN + 1))
                        act.sem_inc(g0_free, 1)
                        nc.scalar.activation(uz[:], uz[:], ACT.Exp, scale=-1.0).then_inc(uz_act, 1)
                        act.wait_ge(uz_act, after(2 * SN + 1))
                        nc.scalar.activation(uz[:], uz[:], ACT.Ln, bias=1.0).then_inc(uz_act, 1)

                    group(0)
                    group(1)
                    if st.inproj:
                        x_taps()
                    if first and st.ffn:
                        rstd(mv2, rstd2, l2_stats, l2_ln, l2_r, c - 1)
                    group(2)
                    if zz and not last:
                        dt_softplus()
                    if last and st.norm1:
                        rstd(mv1, rstd1, l1_stats, l1_ln, l1_r, c + 3)
                    group(3)
                    if st.inproj:
                        x_sigmoid()
                    if zz:
                        z_sigmoid()
                    group(4)
                    if st.inproj:
                        act.wait_ge(mx_dve, after(SX + 1))
                        nc.scalar.activation(ux[:], ux[:], ACT.Exp).then_inc(sx_act, 1)
                    if zz:
                        act.wait_ge(mz_dve, after(SN + 1))
                        nc.scalar.activation(uz[:], uz[:], ACT.Exp).then_inc(sz_act, 1)
                    group(5)
                    if st.outproj:
                        act.wait_ge(o_mm, after(S - PAIRS + 1))
                        act.wait_ge(o_tr, after(S - PAIRS))
                        nc.scalar.copy(ostage[:], g1[:, 0:T]).then_inc(o_evac, 1)
                        act.wait_ge(o_evac, after(S - PAIRS + 1))
                        act.sem_inc(g1_free, 1)
                    group(6)
                    if first and st.ffn:
                        act.wait_ge(f_mm, after(PAIRS * (c - 2)))
                        norm_evac(x2nT, 4 * (c - 2), l2_tr, l2_evac)
                    if last and st.norm1:
                        act.wait_ge(z_mm, after((c + 1) * PAIRS))
                        norm_evac(xnT[:, c % 2], 4 * (c + 2), l1_tr, l1_evac)
                    group(7)
                    if last and st.inproj:
                        act.wait_ge(rms_dve, after(3 * (c + 1) + 3))
                        nc.scalar.activation(ssq[:, 0:2], ssq[:, 0:2], ACT.Ln, bias=eps_rms[:], scale=1.0 / R)
                        nc.scalar.activation(ssq[:, 2:6], ssq[:, 2:6], ACT.Ln, bias=eps_rms[:],
                                             scale=1.0 / N).then_inc(rms_ln, 1)
                        act.wait_ge(rms_ln, after(c + 2))
                        nc.scalar.activation(ssq[:], ssq[:], ACT.Exp, scale=-0.5).then_inc(rms_r, 1)
                        act.wait_ge(ss_tr, after(c + 2))
                        act.wait_ge(dt_mm, after((c + 1) * PAIRS))
                        act.wait_ge(bc_st, landed(c + 1))
                        nc.scalar.activation(ssmT[:], g0[0:E, 0:T], ACT.Identity, scale=lnw[:]).then_inc(ss_evac, 1)
                        act.wait_ge(ss_evac, after(c + 2))
                        act.sem_inc(g0_free, 1)
                        dt_softplus()

                steps(act, step)

            iterations(act, iteration)

        @block.vector
        def _(dve):
            def stats(rows, bst, mv, mid, done, n):
                for tt in range(TT):
                    for h in range(2):
                        ins = nc.vector.bn_stats(bst[:, tt, 6 * h:6 * h + 6], rows(tt, h))
                ins.then_inc(mid, 1)
                dve.wait_ge(mid, after(n))
                dve.sem_inc(aggr_go, 1)
                for tt in range(TT):
                    ins = nc.vector.bn_aggr(mv[:, tt, :], bst[:, tt, :])
                ins.then_inc(done, 1)

            def norm1_stats(chunk):
                dve.wait_ge(xrow_in, landed(chunk + 1))
                stats(lambda tt, h: xrow[:, tt, h * 512:(h + 1) * 512], bst1, mv1, l1_dve, l1_stats, chunk + 1)

            def norm1_apply(chunk):
                dve.wait_ge(l1_r, after(chunk + 1))
                for tt in range(TT):
                    ins = nc.vector.tensor_scalar(xrow[:, tt, :], xrow[:, tt, :], mv1[:, tt, 0:1], rstd1[:, tt:tt + 1],
                                                  ALU.subtract, ALU.mult)
                ins.then_inc(l1_ready, 1)

            dve.wait_ge(a_exp, after(1))
            nc.vector.tensor_scalar(a_neg[:], a_neg[:], -1.0, None, ALU.mult).then_inc(a_ready, 1)
            norm1_stats(0)
            norm1_apply(0)
            dve.wait_ge(zeroed, after(5))

            def iteration(st, c):
                def step(j, first, last):
                    S = c * PAIRS + j
                    SX = S + PAIRS
                    SN = S + 1
                    zz = st.inproj if last else st.scan

                    def group(k, between=()):
                        if st.scan:
                            a, q = divmod(k, NQ)
                            dve.wait_ge(dbxs, after(8 * S + k + 1))
                            dve.wait_ge(hstates, after(8 * S + k))
                            for b in range(2):
                                dve.wait_ge(exps, after(16 * S + 2 * k + b + 1))
                                for i in range(2):
                                    m = 2 * b + i
                                    ins = nc.vector.tensor_tensor_scan(
                                        hps[:, m * T:(m + 1) * T], dA[:, m * T:(m + 1) * T],
                                        dbx[:, k % 2, m * T:(m + 1) * T],
                                        hstate[:, ds((2 * j + a) * N + NQ * q + m, 1)], ALU.mult, ALU.add)
                                ins.then_inc(scans, 1)
                        for f in between:
                            f()
                        if st.scan:
                            dve.wait_ge(scans, after(16 * S + 2 * k + 2))
                            dve.wait_ge(cb_in[q], landed(c + 1))
                            dve.wait_ge(halves, after(8 * S + k - 1))
                            nc.vector.tensor_tensor(hc[:, k % 2, :], hps[:],
                                                    cb[:, NQ * q:NQ * (q + 1), :].rearrange("p n t -> p (n t)"),
                                                    ALU.mult).then_inc(hcs, 1)
                            nc.vector.tensor_copy(hstate[:, ds((2 * j + a) * N + NQ * q, NQ)],
                                                  hps[:, T - 1:GW:T]).then_inc(hstates, 1)

                    def y_gate(SP):
                        dve.wait_ge(sum_mm, after(8 * (SP + 1)))
                        dve.wait_ge(gate_ready, after(SP + 1))
                        for a in range(2):
                            ins = nc.vector.scalar_tensor_tensor(
                                scr[:, a * T:(a + 1) * T], xcs[:, SP % 2, a * T:(a + 1) * T],
                                dparam[:, ds(2 * (SP % PAIRS) + a, 1)],
                                ysum[:, ds((SP % 2) * 2 * T + a * T, T)], ALU.mult, ALU.add)
                        ins.then_inc(y_dve, 1)
                        dve.wait_ge(y_dve, after(SP + 1))
                        dve.wait_ge(o_mm, after(PAIRS * (c - 1)))
                        nc.vector.tensor_tensor(ybuf[:, ds(SP % (2 * PAIRS), 1), :].rearrange("p a t -> p (a t)"),
                                                scr[:], gate[:, SP % 2, :], ALU.mult).then_inc(y_ready, 1)

                    def taps():
                        dve.wait_ge(tap0, after(SX + 1))
                        for i in range(6):
                            tap, a = 1 + i // 2, i % 2
                            if i >= 2:
                                dve.wait_ge(conv, after(6 * SX + i - 1))
                            nc.vector.scalar_tensor_tensor(
                                xcn[:, a * T:(a + 1) * T], xpre[:, a, tap:tap + T],
                                convw[:, ds((2 * j + a) * KC + tap, 1)], xcn[:, a * T:(a + 1) * T],
                                ALU.mult, ALU.add).then_inc(conv, 1)

                    def dt_finish():
                        dve.wait_ge(ld_act, after(2 * SN + 2))
                        nc.vector.tensor_scalar(scr[:], ud[:], 1.0, -1.0, ALU.add, ALU.add).then_inc(dt_dve, 1)
                        dve.wait_ge(dt_dve, after(3 * SN + 1))
                        nc.vector.tensor_tensor(ud[:], ud[:], scr[:], ALU.subtract).then_inc(dt_dve, 1)
                        dve.wait_ge(dt_dve, after(3 * SN + 2))
                        nc.vector.tensor_tensor(ld[:], ld[:], ud[:], ALU.add).then_inc(dt_dve, 1)
                        dve.wait_ge(dt_dve, after(3 * SN + 3))
                        nc.vector.tensor_tensor(dt[:, SN % 2, :], dt[:, SN % 2, :], ld[:], ALU.add
                                                ).then_inc(dt_ready, 1)

                    def x_exponent():
                        dve.wait_ge(ux_act, after(3 * SX + 3))
                        nc.vector.scalar_tensor_tensor(ux[:], xcn[:], 0.0, ux[:], ALU.min, ALU.subtract
                                                       ).then_inc(mx_dve, 1)

                    def z_exponent():
                        dve.wait_ge(uz_act, after(2 * SN + 2))
                        nc.vector.scalar_tensor_tensor(uz[:], gate[:, SN % 2, :], 0.0, uz[:], ALU.min, ALU.subtract
                                                       ).then_inc(mz_dve, 1)

                    def x_silu():
                        dve.wait_ge(sx_act, after(SX + 1))
                        nc.vector.tensor_tensor(xcn[:], xcn[:], ux[:], ALU.mult).then_inc(xc_ready, 1)

                    def z_silu():
                        dve.wait_ge(sz_act, after(SN + 1))
                        nc.vector.tensor_tensor(gate[:, SN % 2, :], gate[:, SN % 2, :], uz[:], ALU.mult
                                                ).then_inc(gate_ready, 1)

                    def block_add(chunk_parity, done, idx, g, free, before):
                        dve.wait_ge(before, after(idx + 1))
                        blk = x2[:, chunk_parity, :].rearrange("p (t h) -> p t h", t=TT)[:, :, ds(j * P, P)]
                        nc.vector.tensor_tensor(blk, g[:, 0:TT * P].rearrange("p (t h) -> p t h", t=TT), blk, ALU.add
                                                ).then_inc(done, 1)
                        dve.wait_ge(done, after(idx + 1))
                        dve.sem_inc(free, 1)

                    def add_out_proj():
                        dve.wait_ge(xres_in, landed(c))
                        block_add((c + 1) % 2, x2_add, S - PAIRS, g1, g1_free, o_tr)

                    def add_ffn():
                        dve.wait_ge(bias_add, after(c - 1))
                        block_add(c % 2, f_add, S - 2 * PAIRS, g1, g1_free, f_mm)

                    def add_x_proj():
                        dve.wait_ge(xp_mm, after(SX + 1))
                        dve.wait_ge(ssm_clear, after(c + 1))
                        nc.vector.tensor_tensor(ssm[:], g0[:, 0:TT * E].rearrange("p (t e) -> p t e", t=TT), ssm[:],
                                                ALU.add).then_inc(xp_add, 1)
                        dve.wait_ge(xp_add, after(SX + 1))
                        dve.sem_inc(g0_free, 1)

                    def rms_norms():
                        sq = scr[:, 0:TT * E].rearrange("p (t e) -> p t e", t=TT)
                        n = 3 * (c + 1)
                        nc.vector.tensor_tensor(sq, ssm[:], ssm[:], ALU.mult).then_inc(rms_dve, 1)
                        dve.wait_ge(rms_dve, after(n + 1))
                        nc.vector.tensor_reduce(ssq[:, 0:2], sq[:, :, 0:R], AX.X, ALU.add).then_inc(rms_dve, 1)
                        nc.vector.tensor_reduce(ssq[:, 2:6].rearrange("p (t g) -> p t g", t=TT),
                                                sq[:, :, R:E].rearrange("p t (g n) -> p t g n", g=2), AX.X, ALU.add
                                                ).then_inc(rms_dve, 1)
                        dve.wait_ge(rms_r, after(c + 2))
                        nc.vector.tensor_tensor(ssn[:, :, 0:R], ssm[:, :, 0:R],
                                                ssq[:, 0:2].unsqueeze(2).to_broadcast([P, TT, R]), ALU.mult)
                        nc.vector.tensor_tensor(ssn[:, :, R:E].rearrange("p t (g n) -> p t g n", g=2),
                                                ssm[:, :, R:E].rearrange("p t (g n) -> p t g n", g=2),
                                                ssq[:, 2:6].rearrange("p (t g) -> p t g", t=TT).unsqueeze(3)
                                                .to_broadcast([P, TT, 2, N]), ALU.mult).then_inc(rms_ready, 1)
                        dve.wait_ge(rms_ready, after(c + 2))
                        nc.vector.memset(ssm[:], 0.0).then_inc(ssm_clear, 1)

                    def norm2_stats():
                        dve.wait_ge(x2_add, after(PAIRS * (c - 1)))
                        rows = x2[:, c % 2, :]
                        stats(lambda tt, h: rows[:, tt * H + h * 512:tt * H + (h + 1) * 512], bst2, mv2, l2_dve,
                              l2_stats, c - 1)

                    def norm2_apply():
                        dve.wait_ge(l2_r, after(c - 1))
                        dve.wait_ge(l1_tr, after(4 * (c + 2) if st.norm1 or isinstance(c, int) and c + 1 < NC else 4 * NC))
                        rows = x2[:, c % 2, :]
                        for tt in range(TT):
                            ins = nc.vector.tensor_scalar(xrow[:, tt, :], rows[:, tt * H:(tt + 1) * H], mv2[:, tt, 0:1],
                                                          rstd2[:, tt:tt + 1], ALU.subtract, ALU.mult)
                        ins.then_inc(l2_ready, 1)
                        for tt in range(TT):
                            ins = nc.vector.tensor_tensor(rows[:, tt * H:(tt + 1) * H],
                                                          rows[:, tt * H:(tt + 1) * H], biasb[:], ALU.add)
                        ins.then_inc(bias_add, 1)

                    def dequantise():
                        dve.wait_ge(codes_in, landed(j + 1))
                        dve.wait_ge(wf_st, landed(j))
                        nc.vector.tensor_scalar(dequant, codes, -ZERO_POINT, None, ALU.add).then_inc(deq_a, 1)
                        dve.wait_ge(deq_a, after(j + 1))
                        dve.wait_ge(scales_in, landed(4 * (j + 1)))
                        nc.vector.tensor_tensor(dequant, dequant, scales, ALU.mult).then_inc(deq_b, 1)

                    if isinstance(c, int) and c == -1:
                        dequantise()
                    group(0, [norm2_stats] if first and st.ffn else [])
                    scan_past = (st.scan and not (first and isinstance(c, int) and c == 0)) or (
                        first and isinstance(c, int) and c == NC)
                    group(1, [lambda: y_gate(S - 1)] if scan_past else [])
                    group(2, ([norm2_apply] if first and st.ffn else [])
                          + ([lambda: norm1_stats(c + 2)] if last and st.norm1 else [])
                          + ([taps] if st.inproj else []))
                    group(3, ([dt_finish] if zz and not last else [])
                          + ([lambda: norm1_apply(c + 2)] if last and st.norm1 else []))
                    group(4, ([x_exponent] if st.inproj else []) + ([z_exponent] if zz else []))
                    group(5, ([x_silu] if st.inproj else []) + ([z_silu] if zz else []))
                    group(6, ([add_out_proj] if st.outproj else []) + ([add_x_proj] if st.inproj else []))
                    group(7, ([add_ffn] if last and st.ffn else [])
                          + ([rms_norms] if last and st.inproj else []))
                    if last and zz:
                        dt_finish()
                    if not last and st.ffn:
                        add_ffn()

                steps(dve, step)

            iterations(dve, iteration)


_IN_SHAPES = None


def _lay_out(inputs):
    import numpy as np

    def arr(name):
        return np.asarray(inputs[name])

    def by_tile(a):
        a = a.reshape(TILES, P, -1)
        return a.transpose(1, 0, 2).reshape(P, -1)

    w = arr("L0_attn_in_proj_w").reshape(KH, P, 2 * PAIRS, 2 * P)
    wo = arr("L0_attn_out_proj_w").reshape(KH, P, TILES, P)
    codes = arr("L0_ffn_q_vals").reshape(KH, P, KH, P)
    scales = arr("L0_ffn_q_scales").reshape(KH, P, KH, P // QB)
    laid = {
        "x": arr("L0_attn_hidden_states").reshape(L, H),
        "win": w.transpose(2, 1, 0, 3).reshape(2 * PAIRS, P, KH * 2 * P),
        "wout": wo.transpose(0, 3, 2, 1).reshape(KH, P, TILES * P),
        "wf_codes": codes.transpose(0, 3, 2, 1).reshape(KH, P, KH * P),
        "wf_scales": scales.transpose(0, 3, 2, 1).reshape(KH, P // QB, KH * P),
        "ffn_bias": arr("L0_ffn_bias"),
        "xproj": by_tile(arr("L0_attn_x_proj_w").T),
        "dtw_in": arr("L0_attn_dt_proj_w").reshape(PAIRS, 2 * P, R).transpose(0, 2, 1),
        "convw_in": by_tile(arr("L0_attn_conv_w")),
        "convb_in": by_tile(arr("L0_attn_conv_b")),
        "dtb_in": by_tile(arr("L0_attn_dt_bias")),
        "alog_in": by_tile(arr("L0_attn_A_log")),
        "dparam_in": by_tile(arr("L0_attn_D_param")),
        "lnw_in": np.concatenate([arr("L0_attn_dt_ln_w"), arr("L0_attn_B_ln_w"), arr("L0_attn_C_ln_w")]).reshape(E, 1),
    }
    return {k: np.ascontiguousarray(v) for k, v in laid.items()}


def kernel(**inputs):
    import concourse.bacc as bacc
    from concourse.bass_utils import run_bass_kernel_spmd

    nc = bacc.Bacc("TRN2", target_bir_lowering=False, num_devices=1)
    laid = _lay_out(inputs)
    arrays = {f"in_{k}": v for k, v in laid.items()}
    args = [nc.dram_tensor(f"in_{k}", v.shape, mybir.dt.from_np(v.dtype), kind="ExternalInput").ap()
            for k, v in laid.items()]
    out = nc.dram_tensor("out_0", (L, H), F32, kind="ExternalOutput").ap()
    build_program(nc, *args, out)
    r = run_bass_kernel_spmd(nc, [arrays], core_ids=[0])
    return r.results[0]["out_0"].reshape(1, L, H)
```
